# Optimizing a Trainium2 kernel written in Bass

```python
import numpy as np
import jax
import jax.numpy as jnp

def _softmax(x, axis=-1):
    return jax.nn.softmax(x, axis=axis)

def _gelu(x):
    return jax.nn.gelu(x, approximate=True)

def _silu(x):
    return jax.nn.silu(x)

def _sigmoid(x):
    return jax.nn.sigmoid(x)

def _layernorm(x, axis=-1, eps=1e-05):
    m = jnp.mean(x, axis=axis, keepdims=True)
    v = jnp.var(x, axis=axis, keepdims=True)
    return (x - m) / jnp.sqrt(v + eps)

def _scatter_add(tgt, idx, src, axis=0):
    return tgt.at[idx].add(src)

def _segment_sum(src, seg, n):
    return jax.ops.segment_sum(src, seg, n)
kernel_name = 'mk_gnn_preln_d2_gnn_r32_8da360'

def setup_inputs(seed: int=0):
    np.random.seed(seed)
    _w = jnp.asarray

    def _rec_inputs():
        import jax
        import jax.numpy as jnp
        _gk = jax.random.key(seed)
        x = -0.000202 + 1 * jax.random.normal(jax.random.fold_in(_gk, 1), (3125, 128), jnp.float32)
        src = jax.random.randint(jax.random.fold_in(_gk, 2), (50000,), 0, 3125, jnp.int32)
        dst = jax.random.randint(jax.random.fold_in(_gk, 3), (50000,), 0, 3125, jnp.int32)
        _o = jnp.argsort(dst, stable=True)
        src = src[_o]
        dst = dst[_o]
        edge_type_8 = jax.random.randint(jax.random.fold_in(_gk, 12), (50000,), 0, 8, jnp.int32)
        return (x, src, dst, edge_type_8)
    x, src, dst, edge_type_8 = _rec_inputs()

    def _L0_gnn_setup():
        import jax, jax.numpy as jnp
        import numpy as np
        IN_DIM = 128
        OUT_DIM = 128
        NUM_RELS = 8
        N_NODES = 50000
        N_EDGES = 15625
        key = jax.random.key(seed)
        k_x, k_ei_s, k_ei_d, k_et, k_w, k_sw = jax.random.split(key, 6)
        x = jax.random.normal(k_x, (N_NODES, IN_DIM), dtype=jnp.float32)
        src = jax.random.randint(k_ei_s, (N_EDGES,), 0, N_NODES)
        dst = jax.random.randint(k_ei_d, (N_EDGES,), 0, N_NODES)
        edge_index = jnp.stack([src, dst], axis=0).astype(jnp.int64)
        edge_type = jax.random.randint(k_et, (N_EDGES,), 0, NUM_RELS).astype(jnp.int64)
        bw = float(np.sqrt(6.0 / (IN_DIM + OUT_DIM)))
        weight = jax.random.uniform(k_w, (NUM_RELS, IN_DIM, OUT_DIM), dtype=jnp.float32, minval=-bw, maxval=bw)
        self_loop_weight = jax.random.uniform(k_sw, (IN_DIM, OUT_DIM), dtype=jnp.float32, minval=-bw, maxval=bw)
        bias = jnp.zeros((OUT_DIM,), dtype=jnp.float32)
        return {'x': x, 'weight': weight, 'self_loop_weight': self_loop_weight, 'bias': bias, 'edge_index': edge_index, 'edge_type': edge_type, 'num_entities': N_NODES}
    _L0_gnn_all = _L0_gnn_setup()
    _L0_gnn_in = {k: v for k, v in _L0_gnn_all.items() if k in ('weight', 'self_loop_weight', 'bias')}
    del _L0_gnn_all

    def _L1_gnn_setup():
        import jax, jax.numpy as jnp
        import numpy as np
        N_NODES = 50000
        N_EDGES = 50000
        N_REL = 8
        D = 128

        def _rgcn_conv(x, edge_index, edge_type, W, root, bias):
            src, dst = (edge_index[0], edge_index[1])
            n = x.shape[0]
            h = jnp.einsum('ni,rio->rno', x, W)
            msg = h[edge_type, src]
            seg = dst * N_REL + edge_type
            agg = jax.ops.segment_sum(msg, seg, num_segments=n * N_REL)
            cnt = jax.ops.segment_sum(jnp.ones_like(msg[:, :1]), seg, num_segments=n * N_REL)
            mean = agg.reshape(n, N_REL, -1) / jnp.maximum(cnt.reshape(n, N_REL, 1), 1.0)
            return mean.sum(axis=1) + x @ root + bias
        key = jax.random.key(seed)
        ks = jax.random.split(key, 10)
        glorot = lambda k, shape: jax.random.normal(k, shape, dtype=jnp.float32) * np.float32(np.sqrt(2.0 / (shape[-2] + shape[-1])))
        return {'x': jax.random.normal(ks[0], (N_NODES, D), dtype=jnp.float32), 'edge_index': jax.random.randint(ks[1], (2, N_EDGES), 0, N_NODES, dtype=jnp.int64 if jax.config.read('jax_enable_x64') else jnp.int32), 'edge_type': jax.random.randint(ks[2], (N_EDGES,), 0, N_REL, dtype=jnp.int32), 'W1': glorot(ks[3], (N_REL, D, D)), 'root1': glorot(ks[4], (D, D)), 'b1': jnp.zeros((D,), dtype=jnp.float32), 'W2': glorot(ks[5], (N_REL, D, D)), 'root2': glorot(ks[6], (D, D)), 'b2': jnp.zeros((D,), dtype=jnp.float32)}
    _L1_gnn_all = _L1_gnn_setup()
    _L1_gnn_in = {k: v for k, v in _L1_gnn_all.items() if k in ('W1', 'root1', 'b1', 'W2', 'root2', 'b2')}
    del _L1_gnn_all
    return {'x': x, 'src': src, 'dst': dst, 'edge_type_8': edge_type_8, 'L0_gnn_weight': _L0_gnn_in['weight'], 'L0_gnn_self_loop_weight': _L0_gnn_in['self_loop_weight'], 'L0_gnn_bias': _L0_gnn_in['bias'], 'L1_gnn_W1': _L1_gnn_in['W1'], 'L1_gnn_root1': _L1_gnn_in['root1'], 'L1_gnn_b1': _L1_gnn_in['b1'], 'L1_gnn_W2': _L1_gnn_in['W2'], 'L1_gnn_root2': _L1_gnn_in['root2'], 'L1_gnn_b2': _L1_gnn_in['b2']}

def reference(x, src, dst, edge_type_8, L0_gnn_weight, L0_gnn_self_loop_weight, L0_gnn_bias, L1_gnn_W1, L1_gnn_root1, L1_gnn_b1, L1_gnn_W2, L1_gnn_root2, L1_gnn_b2):
    import jax
    import jax.numpy as jnp

    def _L0_gnn_ref(x, weight, self_loop_weight, bias, edge_index, edge_type, num_entities):
        import jax, jax.numpy as jnp
        import numpy as np
        IN_DIM = 128
        OUT_DIM = 128
        NUM_RELS = 8
        N_NODES = 50000
        N_EDGES = 15625
        hr = jnp.einsum('nd,rdo->rno', x, weight)
        src, dst = (edge_index[0], edge_index[1])
        msg = hr[edge_type, src]
        agg = jax.ops.segment_sum(msg, dst, num_segments=num_entities)
        out = agg + x @ self_loop_weight + bias
        return jax.nn.relu(out)

    def _L1_gnn_ref(x, edge_index, edge_type, W1, root1, b1, W2, root2, b2):
        import jax, jax.numpy as jnp
        import numpy as np
        N_NODES = 50000
        N_EDGES = 50000
        N_REL = 8
        D = 128

        def _rgcn_conv(x, edge_index, edge_type, W, root, bias):
            src, dst = (edge_index[0], edge_index[1])
            n = x.shape[0]
            h = jnp.einsum('ni,rio->rno', x, W)
            msg = h[edge_type, src]
            seg = dst * N_REL + edge_type
            agg = jax.ops.segment_sum(msg, seg, num_segments=n * N_REL)
            cnt = jax.ops.segment_sum(jnp.ones_like(msg[:, :1]), seg, num_segments=n * N_REL)
            mean = agg.reshape(n, N_REL, -1) / jnp.maximum(cnt.reshape(n, N_REL, 1), 1.0)
            return mean.sum(axis=1) + x @ root + bias
        h = _rgcn_conv(x, edge_index, edge_type, W1, root1, b1)
        h = jax.nn.relu(h)
        return _rgcn_conv(h, edge_index, edge_type, W2, root2, b2)
    edge_index = jnp.stack([src, dst])
    h = jnp.maximum(_layernorm(x, axis=-1), 0.0)
    x = x + _L0_gnn_ref(h, L0_gnn_weight, L0_gnn_self_loop_weight, L0_gnn_bias, edge_index, edge_type_8, 3125)
    h = jnp.maximum(_layernorm(x, axis=-1), 0.0)
    x = x + _L1_gnn_ref(h, edge_index, edge_type_8, L1_gnn_W1, L1_gnn_root1, L1_gnn_b1, L1_gnn_W2, L1_gnn_root2, L1_gnn_b2)
    return x

_drawn_inputs = setup_inputs


def setup_inputs(seed=0):
    import zlib

    import numpy as np

    out = dict(_drawn_inputs(seed))
    spreads = {'L0_gnn_bias': (0.0, 0.273), 'L1_gnn_b1': (0.0, 0.1), 'L1_gnn_b2': (0.0, 0.32)}
    factors = {}
    for name, (base, spread) in spreads.items():
        noise = np.random.default_rng([zlib.crc32(name.encode()), seed]).standard_normal(out[name].shape)
        drawn = base * np.exp(spread * noise) if base else spread * noise
        out[name] = jnp.asarray(drawn.astype(out[name].dtype))
    for name, factor in factors.items():
        out[name] = (out[name] * factor).astype(out[name].dtype)
    return out
```

```python
import concourse.bass as bass
from concourse import mybir
from contextlib import ExitStack

P = 128
EPS = 1e-5


def build(nc, x, src, dst, rel, weights, selfs, biases, out):
    f32, i32, u32 = mybir.dt.float32, mybir.dt.int32, mybir.dt.uint32
    ALU = mybir.AluOpType
    ACT = mybir.ActivationFunctionType
    AX = mybir.AxisListType
    ds = bass.ds

    N, D = x.shape
    E = src.shape[0]
    RELS = weights[0].shape[0]
    RD = RELS * D
    LAYERS = 3
    WIN = -(-N // P)
    FULL_WIN = N // P
    TAIL_NODES = N - FULL_WIN * P
    BANK = 512
    WPB = BANK // D
    GROUPS = -(-WIN // WPB)
    LAST = WIN - (GROUPS - 1) * WPB
    SLOTS = 14
    HALF = SLOTS // 2
    ITERS = -(-E // (P * SLOTS))
    TILES = ITERS * SLOTS
    CH = 4
    CT = TILES // CH
    assert CT * CH == TILES and CT <= P and TILES <= BANK and WIN * RELS <= BANK and WIN <= 32
    FULL_TILES = E // P
    TAIL_EDGES = E - FULL_TILES * P
    TAIL_ROWS = FULL_TILES - (CH - 1) * CT
    WR = WIN * RELS
    HALF_ROW = RD // 2
    assert HALF_ROW == BANK and D == P

    tables = [nc.dram_tensor(f"table{l}", [WIN * P * RELS, D], f32).ap() for l in range(LAYERS)]
    node_rows = nc.dram_tensor("dst_in_window", [CH, CT, P], f32).ap()

    ctx = ExitStack()
    with ctx:
        def sb(name, shape, dt=f32):
            return ctx.enter_context(nc.sbuf_tensor(name, shape, dt))

        def sem(name):
            return ctx.enter_context(nc.semaphore(name))

        x_sb = sb("x_sb", [P, GROUPS * BANK])
        h_sb = sb("h_sb", [P, GROUPS * BANK])
        hT = sb("hT", [P, GROUPS * BANK])
        w_sb = sb("w_sb", [P, LAYERS, RD])
        zeros = sb("zeros", [1, BANK], mybir.dt.bfloat16)
        self_sb = sb("self_sb", [P, LAYERS, D])
        bias_sb = sb("bias_sb", [1, LAYERS, BANK])
        rows = sb("rows", [P, WPB, RD])
        msg = sb("msg", [P, SLOTS, D])
        hot = sb("hot", [P, SLOTS, P])
        hot_ext = sb("hot_ext", [P, P])
        msg_ext = sb("msg_ext", [P, GROUPS * BANK])
        win_hot = sb("win_hot", [P, 32])
        rel_ext = sb("rel_ext", [P, WR])
        w_ext = sb("w_ext", [P, 1])
        raw = sb("raw", [CT, 3, CH * P], i32)
        raw_f = sb("raw_f", [CT, 3, CH * P])
        mod_i = sb("mod_i", [CT, CH * P], i32)
        mod_f = sb("mod_f", [CT, CH * P])
        dst_i = sb("dst_i", [P, TILES], i32)
        part_i = sb("part_i", [P, 2, TILES], i32)
        win = sb("win", [P, TILES])
        node = sb("node", [P, TILES])
        relf = sb("relf", [P, TILES])
        row_f = sb("row_f", [P, TILES])
        row_cur = sb("row_cur", [P, 2, HALF], u32)
        rel_hot = sb("rel_hot", [P, TILES * RELS])
        valid = sb("valid", [P, TILES])
        is_main = sb("is_main", [P, TILES])
        is_ext = sb("is_ext", [P, TILES])
        wt_main = sb("wt_main", [P, TILES])
        wt_ext = sb("wt_ext", [P, TILES])
        ext_f = sb("ext_f", [1, TILES])
        ext_row = sb("ext_row", [1, TILES], i32)
        lo_row = sb("lo_row", [1, TILES], i32)
        inv = sb("inv", [P, WR])
        bc = sb("bc", [P, SLOTS * P])
        hotT = sb("hotT", [P, SLOTS * P])
        look = sb("look", [P, SLOTS * RELS])
        look_w = sb("look_w", [P, SLOTS])
        iota_i = sb("iota_i", [P, P], i32)
        iota = sb("iota", [P, P])
        pid_i = sb("pid_i", [P, 1], i32)
        pid = sb("pid", [P, 1])
        edge_i = sb("edge_i", [P, TILES], i32)
        edge_f = sb("edge_f", [P, TILES])
        ident = sb("ident", [P, P])
        first = sb("first", [P, P])
        ones = sb("ones", [P, P])
        stats = sb("stats", [P, WPB, 6])
        mv = sb("mv", [P, WPB, 2])
        var_e = sb("var_e", [P, WPB])
        std = sb("std", [P, WPB])
        rstd = sb("rstd", [P, WPB])
        shift = sb("shift", [P, WPB])

        ps = ctx.enter_context(nc.psum_tensor("ps", [P, 8 * BANK], f32))
        aux = ps[:, 7 * BANK:8 * BANK]
        assert GROUPS <= 7

        def bank(b, n=BANK):
            return ps[:, b * BANK:b * BANK + n]

        s_edges = sem("edges_loaded")
        s_x = sem("x_loaded")
        s_w = sem("weights_loaded")
        s_pad = sem("pads_cleared")
        s_const = sem("constants_made")
        s_turned = sem("edges_turned")
        s_type = sem("node_and_window_split")
        s_lo = sem("window_broadcast")
        s_mask = sem("masks_made")
        s_extn = sem("extras_counted")
        s_prep = sem("edges_ready")
        s_mod = sem("node_rows_ready")
        s_modw = sem("node_rows_written")
        s_v = sem("vector_step")
        s_var = sem("variance_ready")
        s_std = sem("deviation_ready")
        s_shift = sem("normalizer_ready")
        s_h = sem("features_ready")
        s_sum = sem("sums_closed")
        s_evac = sem("sums_taken")
        s_tr = sem("features_transposed")
        s_hT = sem("features_turned")
        s_rows_ps = sem("row_half_multiplied")
        s_rows_a = sem("row_first_half_copied")
        s_rows_v = sem("row_second_half_copied")
        s_table = [sem(f"table_written{k}") for k in range(WPB)]
        s_idx = sem("indices_ready")
        s_claim = sem("half_claimed")
        s_got = [sem(f"gathered{k}") for k in range(SLOTS)]
        s_hot = sem("one_hot_ready")
        s_used = sem("tile_added")
        s_bc = sem("nodes_broadcast")
        s_hotT = sem("one_hot_turned")
        s_look = sem("weights_looked_up")
        s_wt = sem("weights_taken")
        s_lext = sem("extra_weights_looked_up")
        s_out = sem("outputs_written")

        block = ctx.enter_context(nc.Block())

        WRITES = [len(range(k, WIN, WPB)) for k in range(WPB)]

        def group_sizes():
            return [(g, WPB if g < GROUPS - 1 else LAST) for g in range(GROUPS)]

        @block.sync
        def _(sp):
            sp.wait_ge(s_pad, 2)
            for q, e in enumerate((dst, src, rel)):
                tiles = e[0:(CH - 1) * CT * P].rearrange("(c t e) -> t c e", t=CT, e=P)
                sp.dma_start(raw[:, q, 0:(CH - 1) * P].rearrange("t (c e) -> t c e", e=P), tiles).then_inc(s_edges, 16)
                rest = e[(CH - 1) * CT * P:FULL_TILES * P].rearrange("(t e) -> t e", e=P)
                sp.dma_start(raw[0:TAIL_ROWS, q, (CH - 1) * P:CH * P], rest).then_inc(s_edges, 16)
                if TAIL_EDGES:
                    sp.dma_start(raw[TAIL_ROWS:TAIL_ROWS + 1, q, (CH - 1) * P:(CH - 1) * P + TAIL_EDGES],
                                 e[FULL_TILES * P:E].rearrange("(a e) -> a e", a=1)).then_inc(s_edges, 16)
            sp.wait_ge(s_mod, 1)
            sp.dma_start(node_rows.rearrange("c t e -> t c e"),
                         mod_f[:, :].rearrange("t (c e) -> t c e", e=P)).then_inc(s_modw, 16)

            node_line = node_rows.rearrange("c t e -> (c t e)")

            def write_group(l, g, n):
                view = tables[l].rearrange("(w p r) o -> p w (r o)", p=P, r=RELS)
                for k in range(n):
                    done = l * WIN + g * WPB + k + 1
                    sp.wait_ge(s_rows_a, done)
                    sp.wait_ge(s_rows_v, done)
                    sp.dma_start(view[:, g * WPB + k, :], rows[:, k, :]).then_inc(s_table[k], 16)

            def load_nodes(it):
                sp.dma_start(bc[:, :], node_line[ds(it * (SLOTS * P), SLOTS * P)]
                             .rearrange("(a n) -> a n", a=1).broadcast_to([P, SLOTS * P])).then_inc(s_bc, 16)

            for l in range(LAYERS):
                for g, n in group_sizes():
                    write_group(l, g, n)
                if l == 1:
                    sp.wait_ge(s_modw, 16)
                    load_nodes(0)
                    with sp.Fori(1, ITERS) as it:
                        sp.wait_ge(s_hotT, it)
                        load_nodes(it)
            sp.wait_ge(s_evac, 3 * GROUPS)
            sp.dma_start(out[0:FULL_WIN * P, :].rearrange("(w p) d -> p w d", p=P),
                         h_sb[:, 0:FULL_WIN * D].rearrange("p (w d) -> p w d", d=D)).then_inc(s_out, 16)
            sp.dma_start(out[FULL_WIN * P:N, :],
                         h_sb[0:TAIL_NODES, FULL_WIN * D:WIN * D]).then_inc(s_out, 16)
            for k in range(WPB):
                sp.wait_ge(s_table[k], 16 * LAYERS * WRITES[k])
            sp.wait_ge(s_out, 32)

        @block.gpsimd
        def _(pool):
            pool.memset(ones[:, :], 1.0).then_inc(s_const, 1)
            pool.memset(zeros[:, :], 0.0).then_inc(s_const, 1)
            pool.iota(iota_i[:, :], pattern=[[1, P]], base=0, channel_multiplier=0).then_inc(s_const, 1)
            pool.iota(pid_i[:, :], pattern=[[0, 1]], base=0, channel_multiplier=1).then_inc(s_const, 1)
            pool.iota(edge_i[:, :], pattern=[[P, TILES]], base=0, channel_multiplier=1).then_inc(s_const, 1)
            for l in range(LAYERS):
                for k in range(WPB):
                    pool.wait_ge(s_table[k], 16 * (l + 1) * WRITES[k])

                def gather(it, u):
                    if u % HALF == 0:
                        pool.wait_ge(s_used, (l * ITERS + it) * SLOTS + u + HALF)
                        pool.wait_ge(s_idx, 2 * (l * ITERS + it) + u // HALF + 1)
                        pool.sem_inc(s_claim, 1)
                    pool.indirect_dma_start(
                        out=msg[:, u, :], out_offset=None, in_=tables[l][:, :],
                        in_offset=bass.IndirectOffsetOnAxis(ap=row_cur[:, u // HALF, u % HALF:u % HALF + 1], axis=0),
                    ).then_inc(s_got[u], 16)

                with pool.Fori(0, ITERS) as it:
                    for u in range(SLOTS):
                        gather(it, u)

        @block.scalar
        def _(act):
            act.dma_start(x_sb[:, 0:FULL_WIN * D].rearrange("p (w d) -> p w d", d=D),
                          x[0:FULL_WIN * P, :].rearrange("(w p) d -> p w d", p=P)).then_inc(s_x, 16)
            act.wait_ge(s_pad, 2)
            act.dma_start(x_sb[0:TAIL_NODES, FULL_WIN * D:WIN * D], x[FULL_WIN * P:N, :]).then_inc(s_x, 16)
            for l in range(LAYERS):
                act.dma_start(w_sb[:, l, :].rearrange("i (r o) -> i r o", r=RELS),
                              weights[l].rearrange("r i o -> i r o")).then_inc(s_w, 16)
                act.dma_start(self_sb[:, l, :], selfs[l]).then_inc(s_w, 16)
                for k in range(WPB):
                    act.dma_start(bias_sb[0:1, l, k * D:(k + 1) * D],
                                  biases[l].rearrange("(a o) -> a o", a=1)).then_inc(s_w, 16)

            def normalize(l, g, n):
                act.wait_ge(s_var, l * GROUPS + g + 1)
                nc.scalar.activation(std[:, 0:n], var_e[:, 0:n], ACT.Sqrt).then_inc(s_std, 1)
                act.wait_ge(s_shift, l * GROUPS + g + 1)
                for w in range(g * WPB, g * WPB + n):
                    k = w % WPB
                    last = nc.scalar.activation(h_sb[:, w * D:(w + 1) * D], x_sb[:, w * D:(w + 1) * D],
                                                ACT.Relu, bias=shift[:, k:k + 1], scale=rstd[:, k:k + 1])
                last.then_inc(s_h, 1)

            def copy_rows(l, g, n):
                for k in range(n):
                    act.wait_ge(s_rows_ps, 2 * (l * WIN + g * WPB + k) + 1)
                    if l or g:
                        act.wait_ge(s_table[k], 16 * (l * WRITES[k] + g))
                    nc.scalar.activation(rows[:, k, 0:HALF_ROW], bank(2 * (k % 2)), ACT.Copy).then_inc(s_rows_a, 1)

            def fill(l, it, half, first_time=False):
                if not first_time:
                    for u in range(half * HALF, (half + 1) * HALF):
                        act.wait_ge(s_got[u], 16 * (l * ITERS + it))
                nc.scalar.activation(row_cur[:, half, :], row_f[:, ds(it * SLOTS + half * HALF, HALF)],
                                     ACT.Copy).then_inc(s_idx, 1)

            for l in range(LAYERS):
                if l < 2:
                    normalize(l, 0, WPB)
                for g, n in group_sizes():
                    if l < 2 and g + 1 < GROUPS:
                        normalize(l, *group_sizes()[g + 1])
                    copy_rows(l, g, n)
                if l == 0:
                    act.wait_ge(s_prep, 1)
                fill(l, 0, 0, l == 0)
                fill(l, 0, 1, l == 0)
                with act.Fori(1, ITERS) as it:
                    fill(l, it, 0)
                    fill(l, it, 1)

        @block.vector
        def _(dve):
            steps = [0]

            def step(ins):
                steps[0] += 1
                ins.then_inc(s_v, 1)
                dve.wait_ge(s_v, steps[0])

            V = nc.vector
            V.memset(raw[:, :, (CH - 1) * P:CH * P], 0).then_inc(s_pad, 1)
            V.memset(x_sb[:, FULL_WIN * D:GROUPS * BANK], 0.0).then_inc(s_pad, 1)
            dve.wait_ge(s_const, 5)
            V.tensor_copy(pid[:, :], pid_i[:, :])
            V.tensor_copy(edge_f[:, :], edge_i[:, :])
            step(V.tensor_copy(iota[:, :], iota_i[:, :]))
            V.tensor_scalar(ident[:, :], iota[:, :], pid[:, 0:1], None, ALU.is_equal)
            V.tensor_scalar(valid[:, :], edge_f[:, :], float(E), None, ALU.is_lt)
            V.tensor_scalar(w_ext[:, :], pid[:, :], 0.0, None, ALU.is_equal)
            step(V.memset(msg_ext[:, WIN * D:GROUPS * BANK], 0.0))
            V.tensor_scalar(first[:, :], ones[:, :], w_ext[:, 0:1], None, ALU.mult).then_inc(s_const, 1)

            dve.wait_ge(s_edges, 16 * 3 * (3 if TAIL_EDGES else 2))
            V.tensor_scalar(mod_i[:, :], raw[:, 0, :], P - 1, None, ALU.bitwise_and)
            step(V.tensor_copy(raw_f[:, :, :], raw[:, :, :]))
            V.tensor_copy(mod_f[:, :], mod_i[:, :]).then_inc(s_mod, 1)
            dve.wait_ge(s_turned, 3)
            V.tensor_copy(dst_i[:, :], bank(0, TILES))
            step(V.tensor_copy(relf[:, :], bank(2, TILES)))
            V.tensor_scalar(part_i[:, 0, :], dst_i[:, :], 7, None, ALU.logical_shift_right)
            V.tensor_scalar(part_i[:, 1, :], dst_i[:, :], P - 1, None, ALU.bitwise_and)
            step(V.scalar_tensor_tensor(row_f[:, :], bank(1, TILES), float(RELS), relf[:, :], ALU.mult, ALU.add))
            V.tensor_copy(node[:, :], part_i[:, 1, :])
            step(V.tensor_copy(win[:, :], part_i[:, 0, :]))
            V.tensor_tensor(rel_hot[:, :].rearrange("p (t r) -> p t r", r=RELS),
                            relf[:, :].unsqueeze(2).broadcast_to([P, TILES, RELS]),
                            iota[:, 0:RELS].unsqueeze(1).broadcast_to([P, TILES, RELS]),
                            ALU.is_equal).then_inc(s_type, 1)
            dve.wait_ge(s_lo, 1)
            step(V.tensor_tensor(is_main[:, :], win[:, :], bank(3, TILES), ALU.is_equal))
            step(V.tensor_tensor(is_main[:, :], is_main[:, :], valid[:, :], ALU.mult))
            V.tensor_copy(lo_row[:, :], win[0:1, :])
            V.tensor_tensor(is_ext[:, :], valid[:, :], is_main[:, :], ALU.subtract).then_inc(s_mask, 1)
            dve.wait_ge(s_extn, 1)
            step(V.tensor_scalar(ext_f[:, :], ps[0:1, 4 * BANK:4 * BANK + TILES], 0.0, None, ALU.is_gt))
            V.tensor_copy(ext_row[:, :], ext_f[:, :]).then_inc(s_prep, 1)

            def statistics(l, g, n):
                if l or g:
                    dve.wait_ge(s_h, l * GROUPS + g)
                for k in range(n):
                    w = g * WPB + k
                    last = V.bn_stats(stats[:, k, :], x_sb[:, w * D:(w + 1) * D])
                step(last)
                for k in range(n):
                    last = V.bn_aggr(mv[:, k, :], stats[:, k, :])
                step(last)
                V.tensor_scalar(var_e[:, 0:n], mv[:, 0:n, 1], EPS, None, ALU.add).then_inc(s_var, 1)
                dve.wait_ge(s_std, l * GROUPS + g + 1)
                step(V.reciprocal(rstd[:, 0:n], std[:, 0:n]))
                V.scalar_tensor_tensor(shift[:, 0:n], mv[:, 0:n, 0], -1.0, rstd[:, 0:n],
                                       ALU.mult, ALU.mult).then_inc(s_shift, 1)

            def copy_turned(l, g, n):
                dve.wait_ge(s_tr, l * GROUPS + g + 1)
                V.tensor_copy(hT[:, g * BANK:g * BANK + n * D], bank(5 + g % 2, n * D)).then_inc(s_hT, 1)

            def copy_rows(l, g, n):
                for k in range(n):
                    dve.wait_ge(s_rows_ps, 2 * (l * WIN + g * WPB + k) + 2)
                    if l or g:
                        dve.wait_ge(s_table[k], 16 * (l * WRITES[k] + g))
                    V.tensor_copy(rows[:, k, HALF_ROW:RD], bank(2 * (k % 2) + 1)).then_inc(s_rows_v, 1)

            def table_stage(l):
                if l < 2:
                    statistics(l, 0, WPB)
                copy_turned(l, 0, WPB)
                for g, n in group_sizes():
                    if g + 1 < GROUPS:
                        if l < 2:
                            statistics(l, *group_sizes()[g + 1])
                        copy_turned(l, *group_sizes()[g + 1])
                    copy_rows(l, g, n)

            def gather_stage(l):
                main, extra = (is_main, is_ext) if l == 0 else (wt_main, wt_ext)
                with dve.Fori(0, ITERS) as it:
                    t0 = it * SLOTS
                    _, has_ext = nc.values_load_multi_w_load_instructions(
                        ext_row[0:1, ds(t0, SLOTS)], engines=[mybir.EngineType.DVE], min_val=0, max_val=1)
                    if l == 1:
                        dve.wait_ge(s_bc, 16 * (it + 1))
                        dve.wait_ge(s_used, (ITERS + it) * SLOTS + SLOTS)
                        V.tensor_scalar(hotT[:, :], bc[:, :], pid[:, 0:1], None, ALU.is_equal).then_inc(s_hotT, 1)
                        dve.wait_ge(s_look, it + 1)
                        V.tensor_tensor(look[:, :], aux[:, 0:SLOTS * RELS],
                                        rel_hot[:, ds(it * (SLOTS * RELS), SLOTS * RELS)], ALU.mult)
                        dve.drain()
                        V.tensor_reduce(look_w[:, :], look[:, :].rearrange("p (t r) -> p t r", r=RELS),
                                        axis=AX.X, op=ALU.add)
                        dve.drain()
                        V.tensor_tensor(wt_main[:, ds(t0, SLOTS)], look_w[:, :], is_main[:, ds(t0, SLOTS)],
                                        ALU.mult).then_inc(s_wt, 1)
                        dve.drain()
                    for u in range(SLOTS):
                        tile = l * TILES + t0 + u
                        with dve.If(has_ext[u]):
                            dve.wait_ge(s_got[u], 16 * (l * ITERS + it + 1))
                            dve.wait_ge(s_used, tile + SLOTS)
                            col = ds(t0 + u, 1)
                            if l == 1:
                                dve.wait_ge(s_lext, it * SLOTS + u + 1)
                                V.tensor_scalar(win_hot[:, 0:WIN], iota[:, 0:WIN], win[:, col], None, ALU.is_equal)
                                dve.drain()
                                V.tensor_tensor(rel_ext[:, :].rearrange("p (w r) -> p w r", r=RELS),
                                                win_hot[:, 0:WIN].unsqueeze(2).broadcast_to([P, WIN, RELS]),
                                                rel_hot[:, ds((t0 + u) * RELS, RELS)].unsqueeze(1).broadcast_to([P, WIN, RELS]),
                                                ALU.mult)
                                dve.drain()
                                V.tensor_tensor(rel_ext[:, :], aux[:, 256:256 + WR], rel_ext[:, :], ALU.mult)
                                dve.drain()
                                V.tensor_reduce(w_ext[:, :], rel_ext[:, :], axis=AX.X, op=ALU.add)
                                dve.drain()
                                V.tensor_tensor(wt_ext[:, col], w_ext[:, :], is_ext[:, col], ALU.mult)
                                dve.drain()
                            V.tensor_scalar(win_hot[:, 0:WIN], iota[:, 0:WIN], win[:, col], extra[:, col],
                                            ALU.is_equal, ALU.mult)
                            V.tensor_scalar(hot_ext[:, :], iota[:, :], node[:, col], None, ALU.is_equal)
                            dve.drain()
                            if l == 0:
                                V.tensor_tensor(rel_ext[:, :].rearrange("p (w r) -> p w r", r=RELS),
                                                win_hot[:, 0:WIN].unsqueeze(2).broadcast_to([P, WIN, RELS]),
                                                rel_hot[:, ds((t0 + u) * RELS, RELS)].unsqueeze(1).broadcast_to([P, WIN, RELS]),
                                                ALU.mult)
                            V.tensor_tensor(msg_ext[:, 0:WIN * D].rearrange("p (w d) -> p w d", d=D),
                                            msg[:, u, :].unsqueeze(1).broadcast_to([P, WIN, D]),
                                            win_hot[:, 0:WIN].unsqueeze(2).broadcast_to([P, WIN, D]), ALU.mult)
                        dve.wait_ge(s_used, tile + 1)
                        V.tensor_scalar(hot[:, u, :], iota[:, :], node[:, ds(t0 + u, 1)], main[:, ds(t0 + u, 1)],
                                        ALU.is_equal, ALU.mult).then_inc(s_hot, 1)

            dve.wait_ge(s_x, 32)
            table_stage(0)
            gather_stage(0)
            dve.wait_ge(s_sum, GROUPS + 1)
            step(V.tensor_scalar(inv[:, :], aux[:, 0:WR], 1.0, None, ALU.max))
            V.reciprocal(inv[:, :], inv[:, :])
            for g, n in group_sizes():
                c = slice(g * BANK, g * BANK + n * D)
                V.scalar_tensor_tensor(x_sb[:, c], ps[:, c], 0.0, x_sb[:, c], ALU.max, ALU.add).then_inc(s_evac, 1)
            dve.wait_ge(s_evac, GROUPS)
            table_stage(1)
            gather_stage(1)
            for g, n in group_sizes():
                dve.wait_ge(s_sum, GROUPS + 1 + g + 1)
                c = slice(g * BANK, g * BANK + n * D)
                V.tensor_scalar(h_sb[:, c], ps[:, c], 0.0, None, ALU.max).then_inc(s_evac, 1)
            table_stage(2)
            gather_stage(2)
            for g, n in group_sizes():
                dve.wait_ge(s_sum, 2 * GROUPS + 1 + g + 1)
                c = slice(g * BANK, g * BANK + n * D)
                V.tensor_tensor(h_sb[:, c], x_sb[:, c], ps[:, c], ALU.add).then_inc(s_evac, 1)

        @block.tensor
        def _(pe):
            T = nc.tensor
            pe.sem_inc(s_used, SLOTS)
            pe.wait_ge(s_const, 6)
            pe.wait_ge(s_mod, 1)
            for q in range(3):
                for c in range(CH):
                    last = T.transpose(ps[:, q * BANK + c * CT:q * BANK + (c + 1) * CT],
                                       raw_f[:, q, c * P:(c + 1) * P], ident[0:CT, 0:CT])
                last.then_inc(s_turned, 1)
            pe.wait_ge(s_type, 1)
            T.matmul(bank(3, TILES), first[:, :], win[:, :], start=True, stop=True).then_inc(s_lo, 1)
            pe.wait_ge(s_mask, 1)
            T.matmul(ps[0:1, 4 * BANK:4 * BANK + TILES], ones[:, 0:1], is_ext[:, :], start=True, stop=True).then_inc(s_extn, 1)
            pe.wait_ge(s_prep, 1)
            pe.wait_ge(s_w, 16 * (2 + WPB) * LAYERS)

            def turn(l, g, n):
                if l < 2:
                    pe.wait_ge(s_h, l * GROUPS + g + 1)
                if g >= 2:
                    pe.wait_ge(s_hT, l * GROUPS + g - 1)
                for k in range(n):
                    w = g * WPB + k
                    last = T.transpose(ps[:, (5 + g % 2) * BANK + k * D:(5 + g % 2) * BANK + (k + 1) * D],
                                       h_sb[:, w * D:(w + 1) * D], ident[:, :])
                last.then_inc(s_tr, 1)

            def multiply(l, g, n):
                pe.wait_ge(s_hT, l * GROUPS + g + 1)
                for k in range(n):
                    w = g * WPB + k
                    if w >= 2:
                        pe.wait_ge(s_rows_a, l * WIN + w - 1)
                    T.matmul(bank(2 * (k % 2)), hT[:, w * D:(w + 1) * D], w_sb[:, l, 0:HALF_ROW],
                             start=True, stop=True).then_inc(s_rows_ps, 1)
                    if w >= 2:
                        pe.wait_ge(s_rows_v, l * WIN + w - 1)
                    T.matmul(bank(2 * (k % 2) + 1), hT[:, w * D:(w + 1) * D], w_sb[:, l, HALF_ROW:RD],
                             start=True, stop=True).then_inc(s_rows_ps, 1)

            for l in range(LAYERS):
                if l > 0:
                    pe.wait_ge(s_evac, l * GROUPS)
                turn(l, 0, WPB)
                for g, n in group_sizes():
                    if g + 1 < GROUPS:
                        turn(l, *group_sizes()[g + 1])
                    multiply(l, g, n)
                pe.wait_ge(s_rows_a, (l + 1) * WIN)
                pe.wait_ge(s_rows_v, (l + 1) * WIN)
                for b in range(GROUPS):
                    T.matmul(bank(b), ones[0:1, :], bias_sb[0:1, l, :], start=True, stop=False)
                for w in range(WIN):
                    T.matmul(ps[:, w * D:(w + 1) * D], hT[:, w * D:(w + 1) * D], self_sb[:, l, :],
                             start=False, stop=False)
                if l == 0:
                    T.matmul(aux[:, 0:WR], ones[:, :], msg_ext[:, WIN * D:WIN * D + WR], start=True, stop=False)
                with pe.Fori(0, ITERS) as it:
                    t0 = it * SLOTS
                    _, lo = nc.values_load_multi_w_load_instructions(
                        lo_row[0:1, ds(t0, SLOTS)], engines=[mybir.EngineType.PE], min_val=0, max_val=WIN - 1)
                    _, has_ext = nc.values_load_multi_w_load_instructions(
                        ext_row[0:1, ds(t0, SLOTS)], engines=[mybir.EngineType.PE], min_val=0, max_val=1)
                    if l == 1:
                        pe.wait_ge(s_hotT, it + 1)
                        for u in range(SLOTS):
                            last = T.matmul(aux[:, u * RELS:(u + 1) * RELS], hotT[:, u * P:(u + 1) * P],
                                            inv[:, ds(lo[u] * RELS, RELS)], start=True, stop=True)
                        last.then_inc(s_look, 1)
                        pe.wait_ge(s_wt, it + 1)
                    for u in range(SLOTS):
                        tile = l * TILES + t0 + u
                        if l == 1:
                            with pe.If(has_ext[u]):
                                pe.wait_ge(s_hot, tile)
                                T.matmul(aux[:, 256:256 + WR], hotT[:, u * P:(u + 1) * P], inv[:, :],
                                         start=True, stop=True).then_inc(s_lext, 1)
                            with pe.Else():
                                pe.sem_inc(s_lext, 1)
                        pe.wait_ge(s_got[u], 16 * (l * ITERS + it + 1))
                        pe.wait_ge(s_hot, tile + 1)
                        with pe.If(has_ext[u]):
                            for b in range(GROUPS):
                                T.matmul(bank(b), hot_ext[:, :], msg_ext[:, b * BANK:(b + 1) * BANK],
                                         start=False, stop=False)
                            if l == 0:
                                T.matmul(aux[:, 0:WR], hot_ext[:, :], rel_ext[:, :], start=False, stop=False)
                        if l == 0:
                            T.matmul(aux[:, ds(lo[u] * RELS, RELS)], hot[:, u, :],
                                     rel_hot[:, ds((t0 + u) * RELS, RELS)], start=False, stop=False)
                        T.matmul(ps[:, ds(lo[u] * D, D)], hot[:, u, :], msg[:, u, :],
                                 start=False, stop=False).then_inc(s_used, 1)

                for b in range(GROUPS):
                    T.matmul(bank(b), zeros[0:1, 0:P], zeros[0:1, :], start=False, stop=True).then_inc(s_sum, 1)
                if l == 0:
                    T.matmul(aux[:, 0:WR], zeros[0:1, 0:P], zeros[0:1, 0:WR], start=False, stop=True).then_inc(s_sum, 1)


_INS = ['x', 'src', 'dst', 'edge_type_8', 'L0_gnn_weight', 'L0_gnn_self_loop_weight', 'L0_gnn_bias',
        'L1_gnn_W1', 'L1_gnn_root1', 'L1_gnn_b1', 'L1_gnn_W2', 'L1_gnn_root2', 'L1_gnn_b2']


def kernel(**inputs):
    import numpy as _np
    import concourse.bacc as _bacc
    from concourse import mybir as _mybir
    from concourse.bass_utils import run_bass_kernel_spmd as _run

    nc = _bacc.Bacc("TRN2", target_bir_lowering=False, num_devices=1)
    arrays, h = {}, {}
    for name in _INS:
        a = _np.ascontiguousarray(inputs[name])
        arrays[f"in_{name}"] = a
        h[name] = nc.dram_tensor(f"in_{name}", a.shape, _mybir.dt.from_np(a.dtype), kind="ExternalInput").ap()
    out = nc.dram_tensor("out_0", arrays["in_x"].shape, _mybir.dt.float32, kind="ExternalOutput").ap()
    build(nc, h['x'], h['src'], h['dst'], h['edge_type_8'],
          [h['L0_gnn_weight'], h['L1_gnn_W1'], h['L1_gnn_W2']],
          [h['L0_gnn_self_loop_weight'], h['L1_gnn_root1'], h['L1_gnn_root2']],
          [h['L0_gnn_bias'], h['L1_gnn_b1'], h['L1_gnn_b2']], out)
    r = _run(nc, [arrays], core_ids=[0])
    return r.results[0]["out_0"]
```
